# Optimizing a Trainium2 kernel written in Bass

```python
import numpy as np
import jax
import jax.numpy as jnp

def _softmax(x, axis=-1):
    return jax.nn.softmax(x, axis=axis)

def _gelu(x):
    return jax.nn.gelu(x, approximate=True)

def _silu(x):
    return jax.nn.silu(x)

def _sigmoid(x):
    return jax.nn.sigmoid(x)

def _layernorm(x, axis=-1, eps=1e-05):
    m = jnp.mean(x, axis=axis, keepdims=True)
    v = jnp.var(x, axis=axis, keepdims=True)
    return (x - m) / jnp.sqrt(v + eps)

def _scatter_add(tgt, idx, src, axis=0):
    return tgt.at[idx].add(src)

def _segment_sum(src, seg, n):
    return jax.ops.segment_sum(src, seg, n)
kernel_name = 'mk_dlrm_tower_d1_rec_r8_616f02'

def setup_inputs(seed: int=0):
    np.random.seed(seed)
    _w = jnp.asarray

    def _rec_inputs():
        import jax
        import jax.numpy as jnp
        _tk = jax.random.key(seed)
        dense_ctx = jax.random.normal(jax.random.fold_in(_tk, 190), (2048, 16), jnp.float32)
        ids = jnp.stack([jax.random.randint(jax.random.fold_in(_tk, 200 + f), (2048,), 0, v, jnp.int32) for f, v in enumerate([1250, 1000, 1250, 125000, 1250, 12500, 1000, 1000, 1250, 125000, 1250, 125000, 12500, 12500, 12500, 1250, 1000, 12500, 12500, 1000, 12500, 1250, 1000, 1250, 1000, 1000, 1000, 1250, 1250, 1000, 1000, 1000, 1000, 1250, 1250, 1250, 1250, 1250, 1000, 1250])], axis=1)
        tbl_0 = 0.05 * jax.random.normal(jax.random.fold_in(_tk, 500 + 0), (1250, 64), jnp.float32)
        tbl_1 = 0.05 * jax.random.normal(jax.random.fold_in(_tk, 500 + 1), (1000, 64), jnp.float32)
        tbl_2 = 0.05 * jax.random.normal(jax.random.fold_in(_tk, 500 + 2), (1250, 64), jnp.float32)
        tbl_3 = 0.05 * jax.random.normal(jax.random.fold_in(_tk, 500 + 3), (125000, 64), jnp.float32)
        tbl_4 = 0.05 * jax.random.normal(jax.random.fold_in(_tk, 500 + 4), (1250, 64), jnp.float32)
        tbl_5 = 0.05 * jax.random.normal(jax.random.fold_in(_tk, 500 + 5), (12500, 64), jnp.float32)
        tbl_6 = 0.05 * jax.random.normal(jax.random.fold_in(_tk, 500 + 6), (1000, 64), jnp.float32)
        tbl_7 = 0.05 * jax.random.normal(jax.random.fold_in(_tk, 500 + 7), (1000, 64), jnp.float32)
        tbl_8 = 0.05 * jax.random.normal(jax.random.fold_in(_tk, 500 + 8), (1250, 64), jnp.float32)
        tbl_9 = 0.05 * jax.random.normal(jax.random.fold_in(_tk, 500 + 9), (125000, 64), jnp.float32)
        tbl_10 = 0.05 * jax.random.normal(jax.random.fold_in(_tk, 500 + 10), (1250, 64), jnp.float32)
        tbl_11 = 0.05 * jax.random.normal(jax.random.fold_in(_tk, 500 + 11), (125000, 64), jnp.float32)
        tbl_12 = 0.05 * jax.random.normal(jax.random.fold_in(_tk, 500 + 12), (12500, 64), jnp.float32)
        tbl_13 = 0.05 * jax.random.normal(jax.random.fold_in(_tk, 500 + 13), (12500, 64), jnp.float32)
        tbl_14 = 0.05 * jax.random.normal(jax.random.fold_in(_tk, 500 + 14), (12500, 64), jnp.float32)
        tbl_15 = 0.05 * jax.random.normal(jax.random.fold_in(_tk, 500 + 15), (1250, 64), jnp.float32)
        tbl_16 = 0.05 * jax.random.normal(jax.random.fold_in(_tk, 500 + 16), (1000, 64), jnp.float32)
        tbl_17 = 0.05 * jax.random.normal(jax.random.fold_in(_tk, 500 + 17), (12500, 64), jnp.float32)
        tbl_18 = 0.05 * jax.random.normal(jax.random.fold_in(_tk, 500 + 18), (12500, 64), jnp.float32)
        tbl_19 = 0.05 * jax.random.normal(jax.random.fold_in(_tk, 500 + 19), (1000, 64), jnp.float32)
        tbl_20 = 0.05 * jax.random.normal(jax.random.fold_in(_tk, 500 + 20), (12500, 64), jnp.float32)
        tbl_21 = 0.05 * jax.random.normal(jax.random.fold_in(_tk, 500 + 21), (1250, 64), jnp.float32)
        tbl_22 = 0.05 * jax.random.normal(jax.random.fold_in(_tk, 500 + 22), (1000, 64), jnp.float32)
        tbl_23 = 0.05 * jax.random.normal(jax.random.fold_in(_tk, 500 + 23), (1250, 64), jnp.float32)
        tbl_24 = 0.05 * jax.random.normal(jax.random.fold_in(_tk, 500 + 24), (1000, 64), jnp.float32)
        tbl_25 = 0.05 * jax.random.normal(jax.random.fold_in(_tk, 500 + 25), (1000, 64), jnp.float32)
        tbl_26 = 0.05 * jax.random.normal(jax.random.fold_in(_tk, 500 + 26), (1000, 64), jnp.float32)
        tbl_27 = 0.05 * jax.random.normal(jax.random.fold_in(_tk, 500 + 27), (1250, 64), jnp.float32)
        tbl_28 = 0.05 * jax.random.normal(jax.random.fold_in(_tk, 500 + 28), (1250, 64), jnp.float32)
        tbl_29 = 0.05 * jax.random.normal(jax.random.fold_in(_tk, 500 + 29), (1000, 64), jnp.float32)
        tbl_30 = 0.05 * jax.random.normal(jax.random.fold_in(_tk, 500 + 30), (1000, 64), jnp.float32)
        tbl_31 = 0.05 * jax.random.normal(jax.random.fold_in(_tk, 500 + 31), (1000, 64), jnp.float32)
        tbl_32 = 0.05 * jax.random.normal(jax.random.fold_in(_tk, 500 + 32), (1000, 64), jnp.float32)
        tbl_33 = 0.05 * jax.random.normal(jax.random.fold_in(_tk, 500 + 33), (1250, 64), jnp.float32)
        tbl_34 = 0.05 * jax.random.normal(jax.random.fold_in(_tk, 500 + 34), (1250, 64), jnp.float32)
        tbl_35 = 0.05 * jax.random.normal(jax.random.fold_in(_tk, 500 + 35), (1250, 64), jnp.float32)
        tbl_36 = 0.05 * jax.random.normal(jax.random.fold_in(_tk, 500 + 36), (1250, 64), jnp.float32)
        tbl_37 = 0.05 * jax.random.normal(jax.random.fold_in(_tk, 500 + 37), (1250, 64), jnp.float32)
        tbl_38 = 0.05 * jax.random.normal(jax.random.fold_in(_tk, 500 + 38), (1000, 64), jnp.float32)
        tbl_39 = 0.05 * jax.random.normal(jax.random.fold_in(_tk, 500 + 39), (1250, 64), jnp.float32)
        _rk = jax.random.fold_in(_tk, 7)
        W_top1 = 0.0354441 * jax.random.normal(jax.random.fold_in(_tk, 801), (796, 512), jnp.float32)
        W_top2 = 0.0441942 * jax.random.normal(jax.random.fold_in(_tk, 802), (512, 256), jnp.float32)
        W_top3 = 0.0625 * jax.random.normal(jax.random.fold_in(_tk, 803), (256, 1), jnp.float32)
        b_top1 = jnp.zeros((512,), jnp.float32)
        b_top2 = jnp.zeros((256,), jnp.float32)
        return (dense_ctx, ids, tbl_0, tbl_1, tbl_2, tbl_3, tbl_4, tbl_5, tbl_6, tbl_7, tbl_8, tbl_9, tbl_10, tbl_11, tbl_12, tbl_13, tbl_14, tbl_15, tbl_16, tbl_17, tbl_18, tbl_19, tbl_20, tbl_21, tbl_22, tbl_23, tbl_24, tbl_25, tbl_26, tbl_27, tbl_28, tbl_29, tbl_30, tbl_31, tbl_32, tbl_33, tbl_34, tbl_35, tbl_36, tbl_37, tbl_38, tbl_39, W_top1, b_top1, W_top2, b_top2, W_top3)
    dense_ctx, ids, tbl_0, tbl_1, tbl_2, tbl_3, tbl_4, tbl_5, tbl_6, tbl_7, tbl_8, tbl_9, tbl_10, tbl_11, tbl_12, tbl_13, tbl_14, tbl_15, tbl_16, tbl_17, tbl_18, tbl_19, tbl_20, tbl_21, tbl_22, tbl_23, tbl_24, tbl_25, tbl_26, tbl_27, tbl_28, tbl_29, tbl_30, tbl_31, tbl_32, tbl_33, tbl_34, tbl_35, tbl_36, tbl_37, tbl_38, tbl_39, W_top1, b_top1, W_top2, b_top2, W_top3 = _rec_inputs()

    def _L0_rec_setup():
        import jax, jax.numpy as jnp
        import numpy as np
        B, N, E = (1024, 40, 64)
        P = N * (N - 1) // 2

        def _pair_indices(n):
            row, col = ([], [])
            for i in range(n - 1):
                for j in range(i + 1, n):
                    row.append(i)
                    col.append(j)
            return (np.asarray(row), np.asarray(col))
        key = jax.random.key(seed)
        k1, k2 = jax.random.split(key)
        inputs = jax.random.normal(k1, (B, N, E), dtype=jnp.float32)
        std = float(np.sqrt(2.0 / (E + E)))
        param = jax.random.normal(k2, (E, P, E), dtype=jnp.float32) * std
        return {'inputs': inputs, 'param': param}
    _L0_rec_all = _L0_rec_setup()
    _L0_rec_in = {k: v for k, v in _L0_rec_all.items() if k in ('param',)}
    del _L0_rec_all
    return {'dense_ctx': dense_ctx, 'ids': ids, 'tbl_0': tbl_0, 'tbl_1': tbl_1, 'tbl_2': tbl_2, 'tbl_3': tbl_3, 'tbl_4': tbl_4, 'tbl_5': tbl_5, 'tbl_6': tbl_6, 'tbl_7': tbl_7, 'tbl_8': tbl_8, 'tbl_9': tbl_9, 'tbl_10': tbl_10, 'tbl_11': tbl_11, 'tbl_12': tbl_12, 'tbl_13': tbl_13, 'tbl_14': tbl_14, 'tbl_15': tbl_15, 'tbl_16': tbl_16, 'tbl_17': tbl_17, 'tbl_18': tbl_18, 'tbl_19': tbl_19, 'tbl_20': tbl_20, 'tbl_21': tbl_21, 'tbl_22': tbl_22, 'tbl_23': tbl_23, 'tbl_24': tbl_24, 'tbl_25': tbl_25, 'tbl_26': tbl_26, 'tbl_27': tbl_27, 'tbl_28': tbl_28, 'tbl_29': tbl_29, 'tbl_30': tbl_30, 'tbl_31': tbl_31, 'tbl_32': tbl_32, 'tbl_33': tbl_33, 'tbl_34': tbl_34, 'tbl_35': tbl_35, 'tbl_36': tbl_36, 'tbl_37': tbl_37, 'tbl_38': tbl_38, 'tbl_39': tbl_39, 'W_top1': W_top1, 'b_top1': b_top1, 'W_top2': W_top2, 'b_top2': b_top2, 'W_top3': W_top3, 'L0_rec_param': _L0_rec_in['param']}

def reference(dense_ctx, ids, tbl_0, tbl_1, tbl_2, tbl_3, tbl_4, tbl_5, tbl_6, tbl_7, tbl_8, tbl_9, tbl_10, tbl_11, tbl_12, tbl_13, tbl_14, tbl_15, tbl_16, tbl_17, tbl_18, tbl_19, tbl_20, tbl_21, tbl_22, tbl_23, tbl_24, tbl_25, tbl_26, tbl_27, tbl_28, tbl_29, tbl_30, tbl_31, tbl_32, tbl_33, tbl_34, tbl_35, tbl_36, tbl_37, tbl_38, tbl_39, W_top1, b_top1, W_top2, b_top2, W_top3, L0_rec_param):
    import jax
    import jax.numpy as jnp

    def _L0_rec_ref(inputs, param):
        import jax, jax.numpy as jnp
        import numpy as np
        B, N, E = (1024, 40, 64)
        P = N * (N - 1) // 2

        def _pair_indices(n):
            row, col = ([], [])
            for i in range(n - 1):
                for j in range(i + 1, n):
                    row.append(i)
                    col.append(j)
            return (np.asarray(row), np.asarray(col))
        n = inputs.shape[1]
        rowidx, colidx = _pair_indices(n)
        p = inputs[:, rowidx]
        q = inputs[:, colidx]
        out = jnp.einsum('bie,fie,bif->bi', p, param, q)
        return out[:, None, :]
    e = jnp.stack([tbl_0[ids[:, 0]], tbl_1[ids[:, 1]], tbl_2[ids[:, 2]], tbl_3[ids[:, 3]], tbl_4[ids[:, 4]], tbl_5[ids[:, 5]], tbl_6[ids[:, 6]], tbl_7[ids[:, 7]], tbl_8[ids[:, 8]], tbl_9[ids[:, 9]], tbl_10[ids[:, 10]], tbl_11[ids[:, 11]], tbl_12[ids[:, 12]], tbl_13[ids[:, 13]], tbl_14[ids[:, 14]], tbl_15[ids[:, 15]], tbl_16[ids[:, 16]], tbl_17[ids[:, 17]], tbl_18[ids[:, 18]], tbl_19[ids[:, 19]], tbl_20[ids[:, 20]], tbl_21[ids[:, 21]], tbl_22[ids[:, 22]], tbl_23[ids[:, 23]], tbl_24[ids[:, 24]], tbl_25[ids[:, 25]], tbl_26[ids[:, 26]], tbl_27[ids[:, 27]], tbl_28[ids[:, 28]], tbl_29[ids[:, 29]], tbl_30[ids[:, 30]], tbl_31[ids[:, 31]], tbl_32[ids[:, 32]], tbl_33[ids[:, 33]], tbl_34[ids[:, 34]], tbl_35[ids[:, 35]], tbl_36[ids[:, 36]], tbl_37[ids[:, 37]], tbl_38[ids[:, 38]], tbl_39[ids[:, 39]]], axis=1)
    z = _L0_rec_ref(e, L0_rec_param)
    z = z.reshape(z.shape[0], -1)
    h = jnp.concatenate([z, dense_ctx], axis=1)
    h = jnp.maximum(h @ W_top1 + b_top1, 0.0)
    h = jnp.maximum(h @ W_top2 + b_top2, 0.0)
    y = h @ W_top3
    return y

_drawn_inputs = setup_inputs


def setup_inputs(seed=0):
    import zlib

    import numpy as np

    out = dict(_drawn_inputs(seed))
    spreads = {'b_top1': (0.0, 0.1), 'b_top2': (0.0, 0.1)}
    factors = {}
    for name, (base, spread) in spreads.items():
        noise = np.random.default_rng([zlib.crc32(name.encode()), seed]).standard_normal(out[name].shape)
        drawn = base * np.exp(spread * noise) if base else spread * noise
        out[name] = jnp.asarray(drawn.astype(out[name].dtype))
    for name, factor in factors.items():
        out[name] = (out[name] * factor).astype(out[name].dtype)
    return out
```

```python
from contextlib import ExitStack

import numpy as np

import concourse.bass as bass
from concourse import mybir

F32 = mybir.dt.float32
F32R = mybir.dt.float32r
I32 = mybir.dt.int32
ALU = mybir.AluOpType
ACT = mybir.ActivationFunctionType

P = 128
FIELDS = 40
E = 64
BATCH = 2048
HALVES = 2
HALF = BATCH // HALVES
BT = HALF // P
CH = 512
NCH = HALF // CH
DENSE = 16
H1, H2 = 512, 256

TILES = [(c, k) for c in range(FIELDS) for k in range((c + 1) // 2)]
PAIRS = FIELDS // 2
NT = len(TILES)
GROUP = 4
NG = NT // GROUP
SLOTS = 16
KT = -(-NT // (GROUP * SLOTS))
W_TILES = 4
NW = NT // W_TILES

NAT_SLOTS = 2
U_SLOTS = 2
PROD_SLOTS = 8
PAIR_LAG = 4
RAW_SLOTS = 2
W_SLOTS = 4
WC = W_TILES * P // 2
Q_SLOTS = 2
Q_DMAS = 2

DENSE_ROW = 104
LAST = KT - 1
DMA = 16


def pair_index(r, c):
    return r * (2 * FIELDS - 1 - r) // 2 + c - r - 1


def z_rows():
    rows = np.full((KT, P), -1)
    for i, (c, k) in enumerate(TILES):
        block, j = divmod(i, GROUP * SLOTS)
        slot, group = divmod(j, GROUP)
        for half in range(2):
            if 2 * k + half < c:
                rows[block, 32 * group + 2 * slot + half] = pair_index(2 * k + half, c)
    return rows


def build(nc, tables, ids, w_pairs, w1, b1, w2, b2, w3, dense_t, identity, shifted_ones, out):
    assert NT % GROUP == 0 and NT % W_TILES == 0 and NT % PROD_SLOTS == 0
    assert PAIRS % NAT_SLOTS == 0 and NW % W_SLOTS == 0 and NW % RAW_SLOTS == 0 and PROD_SLOTS == 2 * GROUP

    with ExitStack() as ctx:
        def sb(name, shape, dt=F32):
            return ctx.enter_context(nc.sbuf_tensor(name, shape, dt))

        def ps(name, shape):
            return ctx.enter_context(nc.psum_tensor(name, shape, F32))

        def sem(name):
            return ctx.enter_context(nc.semaphore(name))

        ids_sb = sb("ids_sb", [P, FIELDS * BT], I32)
        nat = sb("nat", [P, NAT_SLOTS, BT, 2, E])
        emb_t = sb("emb_t", [P, FIELDS // 2, HALF])
        pair_parts = sb("pair_parts", [P, 2, HALF], F32R)
        pair_hi, pair_lo = pair_parts[:, 0, :], pair_parts[:, 1, :]
        q_parts = sb("q_parts", [P, Q_SLOTS, 2, HALF], F32R)
        w_raw = sb("w_raw", [P, RAW_SLOTS, WC])
        w_hi = sb("w_hi", [P, RAW_SLOTS, WC], F32R)
        w_lo = sb("w_lo", [P, RAW_SLOTS, WC], F32R)
        w_parts = sb("w_parts", [P, W_SLOTS, W_TILES * P], F32R)
        prod = sb("prod", [P, PROD_SLOTS, HALF])
        z_t = sb("z_t", [P, KT, HALF])
        w1_sb = sb("w1_sb", [P, KT, H1])
        w2_sb = sb("w2_sb", [P, H1 // P, H2])
        w3_sb = sb("w3_sb", [P, H2 // P])
        b1_sb = sb("b1_sb", [P, H1 // P])
        b2_sb = sb("b2_sb", [P, H2 // P])
        ident = sb("ident", [P, P])
        ones = sb("ones", [P, 62])
        h1 = [prod[:, 2 * n:2 * n + 2, :].rearrange("p a (m x) -> p (a m) x", x=CH) for n in range(NCH)]
        y_row = prod[0:1, PROD_SLOTS - 1, 0:CH]
        h2 = [prod[:, 2 * NCH + n, :].rearrange("p (m x) -> p m x", x=CH) for n in range(NCH)]

        u = ps("u", [P, U_SLOTS, NCH, CH])
        e_ps = ps("e_ps", [P, HALF])
        z_ps = ps("z_ps", [P, NCH, CH])
        u_banks = u[:, :, :, :].rearrange("p s n x -> p (s n) x")

        consts_loaded = sem("consts_loaded")
        ids_loaded = sem("ids_loaded")
        mlp_weights_loaded = sem("mlp_weights_loaded")
        dense_loaded = sem("dense_loaded")
        gathered = [sem(f"gathered_{s}") for s in range(NAT_SLOTS)]
        w_raw_loaded = [sem(f"w_raw_loaded_{s}") for s in range(RAW_SLOTS)]
        slot_taken = sem("slot_taken")
        transposed = sem("transposed")
        emb_ready = sem("emb_ready")
        pair_hi_ready = sem("pair_hi_ready")
        pair_lo_ready = sem("pair_lo_ready")
        q_loaded = [sem(f"q_loaded_{s}") for s in range(Q_SLOTS)]
        w_hi_placed = sem("w_hi_placed")
        w_lo_ready = sem("w_lo_ready")
        w_lo_placed = [sem(f"w_lo_placed_{s}") for s in range(W_SLOTS)]
        u_ready = sem("u_ready")
        prod_ready = sem("prod_ready")
        summed = sem("summed")
        z_copied = sem("z_copied")
        pad_set = sem("pad_set")
        h1_ready = sem("h1_ready")
        h1_relu = sem("h1_relu")
        h2_ready = sem("h2_ready")
        h2_relu = sem("h2_relu")
        y_ready = sem("y_ready")
        y_copied = sem("y_copied")
        y_stored = sem("y_stored")

        block = ctx.enter_context(nc.Block())

        def first_tile(c):
            return sum((cc + 1) // 2 for cc in range(c))

        def next_pair(i):
            c, k = TILES[i]
            return c // 2 + 1 if k == 0 and c < FIELDS - 2 and (c == 1 or c % 2 == 0) else 0

        def pair_lo_at(i):
            found = []
            for p in range(1, PAIRS):
                start = first_tile(2 * p - 2)
                for n in range(NCH):
                    at = start + max(min(PAIR_LAG + 2 * n, p - 2), 0)
                    at -= at % 2 if at > start + 1 else 0
                    if at == i:
                        found.append((p, n))
            return found

        def q_loads(half, c):
            a_lap = PAIRS - 1 if c % 2 == 0 else PAIRS
            return half * a_lap + (c // 2 if c % 2 == 0 else c // 2 + 1)

        @block.sync
        def _(sp):
            sp.dma_start(ident[:], identity).then_inc(consts_loaded, DMA)
            sp.dma_start(ones[:], shifted_ones).then_inc(consts_loaded, DMA)
            def load_w(half, lap, j):
                sp.wait_ge(w_lo_ready, lap * NW + max(j - RAW_SLOTS + 1, 0))
                sp.dma_start(w_raw[:, j % RAW_SLOTS, :], w_pairs[j]).then_inc(w_raw_loaded[j % RAW_SLOTS], DMA)

            def place_w_lo(half, lap, j):
                sp.wait_ge(w_lo_ready, lap * NW + j + 1)
                for part in range(2):
                    sp.dma_start(w_parts[E:P, j % W_SLOTS, part * WC:part * WC + WC].bitcast(F32),
                                 w_lo[part * E:part * E + E, j % RAW_SLOTS, :].bitcast(F32)
                                 ).then_inc(w_lo_placed[j % W_SLOTS], DMA)

            def load_q(half, lap, c):
                if c == 1:
                    sp.wait_ge(pair_lo_ready, lap + 1)
                elif c % 2 == 1:
                    sp.wait_ge(u_ready, lap * NT + first_tile(c - 1))
                else:
                    sp.wait_ge(prod_ready, lap * NT + max(first_tile(c - 1), 1))
                own = slice((c % 2) * E, (c % 2) * E + E)
                for to in range(2):
                    sp.dma_start(q_parts[to * E:to * E + E, c % Q_SLOTS, :, :].bitcast(F32),
                                 pair_parts[own, :, :].bitcast(F32)).then_inc(q_loaded[c % Q_SLOTS], DMA)

            with sp.Fori(0, HALVES) as half:
                lap = half + 1
                for j in range(RAW_SLOTS):
                    load_w(half, lap, j)
                for j in range(RAW_SLOTS):
                    place_w_lo(half, lap, j)
                    load_w(half, lap, j + RAW_SLOTS)
                load_q(half, lap, 1)
                for i, (c, k) in enumerate(TILES):
                    if k == 0 and c + 1 < FIELDS:
                        load_q(half, lap, c + 1)
                    j, at = divmod(i, W_TILES)
                    if at == 2 and j + RAW_SLOTS < NW:
                        place_w_lo(half, lap, j + RAW_SLOTS)
                    if at == 2 and j + 2 * RAW_SLOTS < NW:
                        load_w(half, lap, j + 2 * RAW_SLOTS)

        @block.gpsimd
        def _(pool):
            with pool.Fori(0, HALVES) as half:
                lap = half + 1
                pool.wait_ge(transposed, lap * PAIRS)
                pool.dma_start(ids_sb[:], ids[bass.ds(half, 1)].rearrange("a p n -> (a p) n")
                               ).then_inc(ids_loaded, DMA)
                pool.wait_ge(ids_loaded, half * DMA + DMA)
                for c in range(FIELDS):
                    p = c // 2
                    slot = p % NAT_SLOTS
                    if c % 2 == 0:
                        pool.wait_ge(transposed, lap * PAIRS + max(p - NAT_SLOTS + 1, 0))
                        pool.sem_inc(slot_taken, 1)
                    for t in range(BT):
                        col = c * BT + t
                        nc.gpsimd.indirect_dma_start(
                            out=nat[:, slot, t, c % 2, :], out_offset=None, in_=tables[c],
                            in_offset=bass.IndirectOffsetOnAxis(ap=ids_sb[:, col:col + 1], axis=0),
                        ).then_inc(gathered[slot], DMA)

        @block.scalar
        def _(act):
            act.sem_inc(emb_ready, PAIRS)
            act.sem_inc(pair_hi_ready, PAIRS)
            act.sem_inc(w_hi_placed, NW)
            act.sem_inc(z_copied, KT)
            act.sem_inc(h1_relu, NCH * H1 // P)
            act.sem_inc(h2_relu, NCH * H2 // P)
            act.sem_inc(y_copied, NCH)
            act.dma_start(w1_sb[:], w1).then_inc(mlp_weights_loaded, DMA)
            act.dma_start(w2_sb[:], w2).then_inc(mlp_weights_loaded, DMA)
            act.dma_start(w3_sb[:], w3).then_inc(mlp_weights_loaded, DMA)
            act.dma_start(b1_sb[:], b1).then_inc(mlp_weights_loaded, DMA)
            act.dma_start(b2_sb[:], b2).then_inc(mlp_weights_loaded, DMA)
            act.wait_ge(pad_set, 1)
            act.wait_ge(mlp_weights_loaded, 5 * DMA)

            def copy_pair(half, lap, p):
                act.wait_ge(transposed, lap * PAIRS + p + 1)
                if p == 0:
                    act.wait_ge(prod_ready, lap * NT)
                nc.scalar.activation(emb_t[:, p, :], e_ps[:], ACT.Copy).then_inc(emb_ready, 1)
                if p >= 1:
                    for c in (2 * p - 2, 2 * p - 1):
                        if c > 0:
                            act.wait_ge(q_loaded[c % Q_SLOTS], q_loads(half, c) * Q_DMAS * DMA)
                nc.scalar.activation(pair_hi, e_ps[:], ACT.Copy).then_inc(pair_hi_ready, 1)

            def split_w(half, lap, j):
                raw = w_raw[:, j % RAW_SLOTS, :]
                act.wait_ge(w_raw_loaded[j % RAW_SLOTS], (half * (NW // RAW_SLOTS) + j // RAW_SLOTS + 1) * DMA)
                nc.scalar.activation(w_hi[:, j % RAW_SLOTS, :], raw, ACT.Copy)
                act.wait_ge(u_ready, lap * NT + max(j - W_SLOTS + 1, 0) * W_TILES)
                for part in range(2):
                    ins = nc.scalar.activation(w_parts[0:E, j % W_SLOTS, part * WC:part * WC + WC],
                                               raw[part * E:part * E + E, :], ACT.Copy)
                ins.then_inc(w_hi_placed, 1)

            def copy_z(half, lap, block_of_z):
                act.wait_ge(summed, lap * NG + min((block_of_z + 1) * SLOTS, NG))
                if block_of_z == 0:
                    act.wait_ge(h1_ready, lap * (NCH * H1 // P))
                rows = slice(0, DENSE_ROW if block_of_z == LAST else P)
                nc.scalar.activation(z_t[rows, block_of_z, :], z_ps[rows, :, :], ACT.Copy
                                     ).then_inc(z_copied, 1)

            with act.Fori(0, HALVES) as half:
                lap = half + 1
                act.dma_start(z_t[DENSE_ROW:DENSE_ROW + DENSE, LAST, :],
                              dense_t[:, bass.ds(half * HALF, HALF)]).then_inc(dense_loaded, DMA)
                for j in range(RAW_SLOTS):
                    split_w(half, lap, j)
                copy_pair(half, lap, 0)
                for i, (c, k) in enumerate(TILES):
                    if i % W_TILES == 0 and i // W_TILES + RAW_SLOTS < NW:
                        split_w(half, lap, i // W_TILES + RAW_SLOTS)
                    if next_pair(i):
                        copy_pair(half, lap, next_pair(i))
                    g, at = divmod(i, GROUP)
                    if at == 3 and g >= 1 and g % SLOTS == 0:
                        copy_z(half, lap, g // SLOTS - 1)
                copy_z(half, lap, LAST)
                for n in range(NCH):
                    for m in range(H1 // P):
                        act.wait_ge(h1_ready, lap * (NCH * H1 // P) + n * (H1 // P) + m + 1)
                        nc.scalar.activation(h1[n][:, m, :], u_banks[:, m, :], ACT.Relu, bias=b1_sb[:, m:m + 1]
                                             ).then_inc(h1_relu, 1)
                    for m in range(H2 // P):
                        act.wait_ge(h2_ready, lap * (NCH * H2 // P) + n * (H2 // P) + m + 1)
                        nc.scalar.activation(h2[n][:, m, :], e_ps[:, m * CH:m * CH + CH], ACT.Relu,
                                             bias=b2_sb[:, m:m + 1]).then_inc(h2_relu, 1)
                    act.wait_ge(y_ready, lap * NCH + n + 1)
                    nc.scalar.activation(y_row, z_ps[0:1, n, :], ACT.Copy).then_inc(y_copied, 1)
                    act.wait_ge(y_copied, lap * NCH + n + 1)
                    act.dma_start(out[:, bass.ds(half * HALF + n * CH, CH)], y_row).then_inc(y_stored, DMA)
                    act.wait_ge(y_stored, (half * NCH + n + 1) * DMA)

        @block.vector
        def _(dve):
            dve.sem_inc(pair_lo_ready, 1)
            dve.sem_inc(w_lo_ready, NW)
            dve.sem_inc(prod_ready, NT)
            nc.vector.memset(z_t[96:P, LAST, :], 0.0).then_inc(pad_set, 1)

            def lo_of_pair(half, lap, p, n):
                if n == 0:
                    dve.wait_ge(pair_hi_ready, lap * PAIRS + p + 1)
                cols = slice(n * CH, n * CH + CH)
                ins = nc.vector.tensor_tensor(pair_lo[:, cols], emb_t[:, p, cols], pair_hi[:, cols].bitcast(F32),
                                              ALU.subtract)
                if p == 0 and n == NCH - 1:
                    ins.then_inc(pair_lo_ready, 1)

            def lo_of_w(half, lap, j):
                dve.wait_ge(w_hi_placed, lap * NW + j + 1)
                if j >= RAW_SLOTS:
                    i = j - RAW_SLOTS
                    dve.wait_ge(w_lo_placed[i % W_SLOTS], (half * (NW // W_SLOTS) + i // W_SLOTS + 1) * 2 * DMA)
                nc.vector.tensor_tensor(w_lo[:, j % RAW_SLOTS, :], w_raw[:, j % RAW_SLOTS, :],
                                        w_hi[:, j % RAW_SLOTS, :].bitcast(F32), ALU.subtract
                                        ).then_inc(w_lo_ready, 1)

            with dve.Fori(0, HALVES) as half:
                lap = half + 1
                for j in range(RAW_SLOTS):
                    lo_of_w(half, lap, j)
                for n in range(NCH):
                    lo_of_pair(half, lap, 0, n)
                for i, (c, k) in enumerate(TILES):
                    for p, n in pair_lo_at(i):
                        lo_of_pair(half, lap, p, n)
                    if k == 0:
                        dve.wait_ge(emb_ready, lap * PAIRS + c // 2 + 1)
                    if i % GROUP == 0:
                        dve.wait_ge(summed, lap * NG + max(i // GROUP - 1, 0))
                    dve.wait_ge(u_ready, lap * NT + i + 1)
                    nc.vector.tensor_tensor(prod[:, i % PROD_SLOTS, :],
                                            u[:, i % U_SLOTS, :, :].rearrange("p n x -> p (n x)"),
                                            emb_t[:, k, :], ALU.mult).then_inc(prod_ready, 1)
                    if i % W_TILES == 1 and i // W_TILES + RAW_SLOTS < NW:
                        lo_of_w(half, lap, i // W_TILES + RAW_SLOTS)

        @block.tensor
        def _(pe):
            pe.sem_inc(transposed, PAIRS)
            pe.sem_inc(u_ready, NT)
            pe.sem_inc(summed, NG)
            pe.sem_inc(h1_ready, NCH * H1 // P)
            pe.sem_inc(h2_ready, NCH * H2 // P)
            pe.sem_inc(y_ready, NCH)
            pe.wait_ge(consts_loaded, 2 * DMA)

            def transpose_pair(half, lap, p):
                slot = p % NAT_SLOTS
                pe.wait_ge(gathered[slot], (half * (PAIRS // NAT_SLOTS) + p // NAT_SLOTS + 1) * (2 * BT * DMA))
                pe.wait_ge(pair_hi_ready, lap * PAIRS + p)
                if p == 0:
                    pe.wait_ge(h2_relu, lap * (NCH * H2 // P))
                for t in range(BT):
                    mm = nc.tensor.transpose(e_ps[:, t * P:t * P + P],
                                             nat[:, slot, t, :, :].rearrange("p a e -> p (a e)"), ident[:])
                mm.then_inc(transposed, 1)

            def contract(half, lap, i):
                c, k = TILES[i]
                j, at = divmod(i, W_TILES)
                if at == 0:
                    pe.wait_ge(w_hi_placed, lap * NW + j + 1)
                    pe.wait_ge(w_lo_placed[j % W_SLOTS], (half * (NW // W_SLOTS) + j // W_SLOTS + 1) * 2 * DMA)
                if k == 0:
                    pe.wait_ge(q_loaded[c % Q_SLOTS], q_loads(half, c) * Q_DMAS * DMA)
                pe.wait_ge(prod_ready, lap * NT + max(i - U_SLOTS + 1, 0))
                w = w_parts[:, j % W_SLOTS, at * P:at * P + P]
                for n in range(NCH):
                    cols = slice(n * CH, n * CH + CH)
                    nc.tensor.matmul(u[:, i % U_SLOTS, n, :], w, q_parts[:, c % Q_SLOTS, 0, cols],
                                     start=True, stop=False)
                    mm = nc.tensor.matmul(u[:, i % U_SLOTS, n, :], w, q_parts[:, c % Q_SLOTS, 1, cols],
                                          start=False, stop=True)
                mm.then_inc(u_ready, 1)

            def sum_group(half, lap, g, n):
                block_of_z, slot = divmod(g, SLOTS)
                if n == 0:
                    pe.wait_ge(prod_ready, lap * NT + GROUP * (g + 1))
                if n == 0 and slot == 0:
                    pe.wait_ge(z_copied, lap * KT + block_of_z)
                    if block_of_z == 0:
                        pe.wait_ge(y_copied, lap * NCH)
                last = slot == SLOTS - 1 or g == NG - 1
                for a in range(GROUP):
                    mm = nc.tensor.matmul(z_ps[32 * a:32 * a + 32, n, :], ones[:, 30 - 2 * slot:62 - 2 * slot],
                                          prod[:, (GROUP * g + a) % PROD_SLOTS, n * CH:n * CH + CH],
                                          start=(slot == 0), stop=last)
                if n == NCH - 1:
                    mm.then_inc(summed, 1)

            def mlp(half, lap):
                pe.wait_ge(mlp_weights_loaded, 5 * DMA)
                pe.wait_ge(z_copied, lap * KT + KT)
                pe.wait_ge(dense_loaded, half * DMA + DMA)
                pe.wait_ge(prod_ready, lap * NT + NT)
                pe.wait_ge(pair_hi_ready, lap * PAIRS + PAIRS)
                for n in range(NCH):
                    cols = slice(n * CH, n * CH + CH)
                    for m in range(H1 // P):
                        if n >= 1:
                            pe.wait_ge(h1_relu, lap * (NCH * H1 // P) + (n - 1) * (H1 // P) + m + 1)
                        for j in range(KT):
                            mm = nc.tensor.matmul(u_banks[:, m, :], w1_sb[:, j, m * P:m * P + P],
                                                  z_t[:, j, cols], start=(j == 0), stop=(j == KT - 1))
                        mm.then_inc(h1_ready, 1)
                    for m in range(H2 // P):
                        if n >= 1:
                            pe.wait_ge(h2_relu, lap * (NCH * H2 // P) + (n - 1) * (H2 // P) + m + 1)
                        for j in range(H1 // P):
                            if m == 0:
                                pe.wait_ge(h1_relu, lap * (NCH * H1 // P) + n * (H1 // P) + j + 1)
                            mm = nc.tensor.matmul(e_ps[:, m * CH:m * CH + CH], w2_sb[:, j, m * P:m * P + P],
                                                  h1[n][:, j, :], start=(j == 0), stop=(j == H1 // P - 1))
                        mm.then_inc(h2_ready, 1)
                    for j in range(H2 // P):
                        pe.wait_ge(h2_relu, lap * (NCH * H2 // P) + n * (H2 // P) + j + 1)
                        mm = nc.tensor.matmul(z_ps[0:1, n, :], w3_sb[:, j:j + 1], h2[n][:, j, :],
                                              start=(j == 0), stop=(j == H2 // P - 1))
                    mm.then_inc(y_ready, 1)

            with pe.Fori(0, HALVES) as half:
                lap = half + 1
                transpose_pair(half, lap, 0)
                for i, (c, k) in enumerate(TILES):
                    contract(half, lap, i)
                    if next_pair(i):
                        transpose_pair(half, lap, next_pair(i))
                    g, at = divmod(i, GROUP)
                    g, at = divmod(i, GROUP)
                    if at % 2 == 1 and g >= 1:
                        sum_group(half, lap, g - 1, at // 2)
                for n in range(NCH):
                    sum_group(half, lap, NG - 1, n)
                mlp(half, lap)


def kernel(**inputs):
    import concourse.bacc as bacc
    from concourse.bass_utils import run_bass_kernel_spmd

    a = {k: np.ascontiguousarray(v) for k, v in inputs.items()}

    param = np.concatenate([a["L0_rec_param"], np.zeros((E, 1, E), np.float32)], axis=1)
    order = [pair_index(2 * k + h, c) if 2 * k + h < c else -1 for c, k in TILES for h in range(2)]
    w_pairs = param[:, order, :].reshape(E, NW, 2, WC).transpose(1, 2, 0, 3).reshape(NW, P, WC)

    rows = z_rows()
    w1_ext = np.concatenate([a["W_top1"], np.zeros((1, H1), np.float32)], axis=0)
    rows[LAST, DENSE_ROW:DENSE_ROW + DENSE] = FIELDS * (FIELDS - 1) // 2 + np.arange(DENSE)
    w1 = w1_ext[rows].transpose(1, 0, 2)

    shifted_ones = np.zeros((P, 62), np.float32)
    shifted_ones[:E, 30] = shifted_ones[E:, 31] = 1.0

    arrays = {f"tbl_{c}": a[f"tbl_{c}"] for c in range(FIELDS)}
    arrays |= {
        "ids": a["ids"].reshape(HALVES, BT, P, FIELDS).transpose(0, 2, 3, 1).reshape(HALVES, P, FIELDS * BT),
        "w_pairs": w_pairs,
        "w1": w1,
        "b1": a["b_top1"].reshape(H1 // P, P).T,
        "w2": a["W_top2"].reshape(H1 // P, P, H2).transpose(1, 0, 2),
        "b2": a["b_top2"].reshape(H2 // P, P).T,
        "w3": a["W_top3"].reshape(H2 // P, P).T,
        "dense_t": a["dense_ctx"].T,
        "identity": np.eye(P, dtype=np.float32),
        "shifted_ones": shifted_ones,
    }
    nc = bacc.Bacc("TRN2", target_bir_lowering=False, num_devices=1)
    feeds, aps = {}, {}
    for name, array in arrays.items():
        array = np.ascontiguousarray(array)
        feeds[f"in_{name}"] = array
        aps[name] = nc.dram_tensor(f"in_{name}", array.shape, mybir.dt.from_np(array.dtype),
                                   kind="ExternalInput").ap()
    out = nc.dram_tensor("y", (1, BATCH), F32, kind="ExternalOutput").ap()
    tables = [aps.pop(f"tbl_{c}") for c in range(FIELDS)]
    build(nc, tables, out=out, **aps)
    r = run_bass_kernel_spmd(nc, [feeds], core_ids=[0])
    return r.results[0]["y"].reshape(BATCH, 1)
```

```python
from contextlib import ExitStack

import numpy as np

import concourse.bass as bass
from concourse import mybir

F32 = mybir.dt.float32
F32R = mybir.dt.float32r
I32 = mybir.dt.int32
ALU = mybir.AluOpType
ACT = mybir.ActivationFunctionType

P = 128
FIELDS = 40
E = 64
BATCH = 2048
HALVES = 2
HALF = BATCH // HALVES
BT = HALF // P
CH = 512
NCH = HALF // CH
DENSE = 16
H1, H2 = 512, 256

TILES = [(c, k) for c in range(FIELDS) for k in range((c + 1) // 2)]
PAIRS = FIELDS // 2
NT = len(TILES)
GROUP = 4
NG = NT // GROUP
SLOTS = 16
KT = -(-NT // (GROUP * SLOTS))
W_TILES = 4
NW = NT // W_TILES

NAT_SLOTS = 2
AHEAD = 8
GATHER_SEMS = NAT_SLOTS + AHEAD
U_SLOTS = 2
PROD_SLOTS = 8
Q_LEAD = 4
PAIR_LEAD = 2
RAW_SLOTS = 2
W_SLOTS = 4
WC = W_TILES * P // 2
Q_SLOTS = 3

DENSE_ROW = 104
LAST = KT - 1
DMA = 16


def pair_index(r, c):
    return r * (2 * FIELDS - 1 - r) // 2 + c - r - 1


def z_rows():
    rows = np.full((KT, P), -1)
    for i, (c, k) in enumerate(TILES):
        block, j = divmod(i, GROUP * SLOTS)
        slot, group = divmod(j, GROUP)
        for half in range(2):
            if 2 * k + half < c:
                rows[block, 32 * group + 2 * slot + half] = pair_index(2 * k + half, c)
    return rows


def build(nc, tables, ids, w_pairs, w1, b1, w2, b2, w3, dense_t, identity, shifted_ones, out):
    assert NT % GROUP == 0 and NT % W_TILES == 0 and NT % PROD_SLOTS == 0
    assert (FIELDS - 1) % Q_SLOTS == 0 and PAIRS == 2 * GATHER_SEMS and NW % W_SLOTS == 0 and NW % RAW_SLOTS == 0 and PROD_SLOTS == 2 * GROUP

    with ExitStack() as ctx:
        def sb(name, shape, dt=F32):
            return ctx.enter_context(nc.sbuf_tensor(name, shape, dt))

        def ps(name, shape):
            return ctx.enter_context(nc.psum_tensor(name, shape, F32))

        def sem(name):
            return ctx.enter_context(nc.semaphore(name))

        ids_sb = sb("ids_sb", [P, FIELDS * BT], I32)
        nat = sb("nat", [P, NAT_SLOTS, BT, 2, E])
        emb_t = sb("emb_t", [P, FIELDS // 2, HALF])
        q_parts = sb("q_parts", [P, Q_SLOTS, 2, HALF], F32R)
        w_raw = sb("w_raw", [P, RAW_SLOTS, WC])
        w_hi = sb("w_hi", [P, RAW_SLOTS, WC], F32R)
        w_lo = sb("w_lo", [P, RAW_SLOTS, WC], F32R)
        w_parts = sb("w_parts", [P, W_SLOTS, W_TILES * P], F32R)
        prod = sb("prod", [P, PROD_SLOTS, HALF])
        z_t = sb("z_t", [P, KT, HALF])
        w1_sb = sb("w1_sb", [P, KT, H1])
        w2_sb = sb("w2_sb", [P, H1 // P, H2])
        w3_sb = sb("w3_sb", [P, H2 // P])
        b1_sb = sb("b1_sb", [P, H1 // P])
        b2_sb = sb("b2_sb", [P, H2 // P])
        ident = sb("ident", [P, P])
        ones = sb("ones", [P, 62])
        h1 = [prod[:, 2 * n:2 * n + 2, :].rearrange("p a (m x) -> p (a m) x", x=CH) for n in range(NCH)]
        y_rows = [prod[0:1, 3 * NCH + n, 0:CH] for n in range(NCH)]
        h2 = [prod[:, 2 * NCH + n, :].rearrange("p (m x) -> p m x", x=CH) for n in range(NCH)]

        u = ps("u", [P, U_SLOTS, NCH, CH])
        e_ps = ps("e_ps", [P, HALF])
        z_ps = ps("z_ps", [P, NCH, CH])
        u_banks = u[:, :, :, :].rearrange("p s n x -> p (s n) x")

        consts_loaded = sem("consts_loaded")
        ids_loaded = sem("ids_loaded")
        mlp_weights_loaded = sem("mlp_weights_loaded")
        dense_loaded = sem("dense_loaded")
        gathered = [sem(f"gathered_{s}") for s in range(GATHER_SEMS)]
        w_raw_loaded = [sem(f"w_raw_loaded_{s}") for s in range(RAW_SLOTS)]
        slot_taken = sem("slot_taken")
        transposed = sem("transposed")
        emb_ready = sem("emb_ready")
        q_hi_ready = sem("q_hi_ready")
        q_lo_ready = sem("q_lo_ready")
        q_loaded = [sem(f"q_loaded_{s}") for s in range(Q_SLOTS)]
        w_hi_placed = sem("w_hi_placed")
        w_lo_ready = sem("w_lo_ready")
        w_lo_placed = [sem(f"w_lo_placed_{s}") for s in range(W_SLOTS)]
        u_ready = sem("u_ready")
        prod_ready = sem("prod_ready")
        summed = sem("summed")
        z_copied = sem("z_copied")
        pad_set = sem("pad_set")
        h1_ready = sem("h1_ready")
        h1_relu = sem("h1_relu")
        h2_ready = sem("h2_ready")
        h2_relu = sem("h2_relu")
        y_ready = sem("y_ready")
        y_copied = sem("y_copied")
        y_stored = sem("y_stored")

        block = ctx.enter_context(nc.Block())

        def first_tile(c):
            return sum((cc + 1) // 2 for cc in range(c))

        def gathered_rows(p):
            if NAT_SLOTS <= p < GATHER_SEMS:
                return emb_t[:, p + PAIRS - GATHER_SEMS, :].rearrange("p (t a e) -> p t a e", a=2, e=E)
            return nat[:, p % NAT_SLOTS, :, :, :]

        def split_step(c):
            return 4 if c >= 14 else 2 if c >= 8 else 1

        def split_at(c, n):
            step = split_step(c)
            first = first_tile(c) - Q_LEAD - (NCH - 1) * step
            return max(first - first % step, first_tile(c - 2)) + n * step

        def pair_at(p):
            return max(split_at(2 * p, 0) - PAIR_LEAD, 0)

        pairs_at = {i: [p for p in range(2, PAIRS) if pair_at(p) == i] for i in range(NT)}
        fields_at = {i: [(c, n) for c in range(4, FIELDS) for n in range(NCH) if split_at(c, n) == i]
                     for i in range(NT)}

        def own(c):
            return slice((c % 2) * E, (c % 2) * E + E)

        def q_loads(half, c):
            return half * ((FIELDS - 1) // Q_SLOTS) + (c - 1) // Q_SLOTS + 1

        @block.sync
        def _(sp):
            sp.dma_start(ident[:], identity).then_inc(consts_loaded, DMA)
            sp.dma_start(ones[:], shifted_ones).then_inc(consts_loaded, DMA)
            def load_w(half, lap, j):
                sp.wait_ge(w_lo_ready, lap * NW + max(j - RAW_SLOTS + 1, 0))
                sp.dma_start(w_raw[:, j % RAW_SLOTS, :], w_pairs[j]).then_inc(w_raw_loaded[j % RAW_SLOTS], DMA)

            def place_w_lo(half, lap, j):
                sp.wait_ge(w_lo_ready, lap * NW + j + 1)
                for part in range(2):
                    sp.dma_start(w_parts[E:P, j % W_SLOTS, part * WC:part * WC + WC].bitcast(F32),
                                 w_lo[part * E:part * E + E, j % RAW_SLOTS, :].bitcast(F32)
                                 ).then_inc(w_lo_placed[j % W_SLOTS], DMA)

            def load_q(half, lap, c):
                sp.wait_ge(q_lo_ready, lap * (FIELDS - 1) + c)
                sp.dma_start(q_parts[own(c + 1), c % Q_SLOTS, :, :].bitcast(F32),
                             q_parts[own(c), c % Q_SLOTS, :, :].bitcast(F32)).then_inc(q_loaded[c % Q_SLOTS], DMA)

            def start(half, lap):
                for j in range(RAW_SLOTS):
                    load_w(half, lap, j)
                load_q(half, lap, 1)
                place_w_lo(half, lap, 0)
                load_w(half, lap, RAW_SLOTS)
                load_q(half, lap, 2)
                place_w_lo(half, lap, 1)
                load_w(half, lap, RAW_SLOTS + 1)
                load_q(half, lap, 3)

            start(0, 1)
            with sp.Fori(0, HALVES) as half:
                lap = half + 1
                for i in range(NT):
                    j, at = divmod(i, W_TILES)
                    if at == 2 and j + RAW_SLOTS < NW:
                        place_w_lo(half, lap, j + RAW_SLOTS)
                    if at == 2 and j + 2 * RAW_SLOTS < NW:
                        load_w(half, lap, j + 2 * RAW_SLOTS)
                    for c, n in fields_at[i]:
                        if n == NCH - 1:
                            load_q(half, lap, c)
                start(half + 1, lap + 1)
            for slot in range(RAW_SLOTS):
                sp.wait_ge(w_raw_loaded[slot], (HALVES * (NW // RAW_SLOTS) + 2) * DMA)
                sp.wait_ge(w_lo_placed[slot], (HALVES * (NW // W_SLOTS) + 1) * 2 * DMA)
            for c in (1, 2, 3):
                sp.wait_ge(q_loaded[c % Q_SLOTS], q_loads(HALVES, c) * DMA)

        @block.gpsimd
        def _(pool):
            def gather_pair(p):
                pool.sem_inc(slot_taken, 1)
                rows = gathered_rows(p)
                for c in (2 * p, 2 * p + 1):
                    for t in range(BT):
                        col = c * BT + t
                        nc.gpsimd.indirect_dma_start(
                            out=rows[:, t, c % 2, :], out_offset=None, in_=tables[c],
                            in_offset=bass.IndirectOffsetOnAxis(ap=ids_sb[:, col:col + 1], axis=0),
                        ).then_inc(gathered[p % GATHER_SEMS], DMA)

            def start(half, lap):
                pool.wait_ge(transposed, lap * PAIRS)
                pool.dma_start(ids_sb[:], ids[bass.ds(half, 1)].rearrange("a p n -> (a p) n")
                               ).then_inc(ids_loaded, DMA)
                pool.wait_ge(ids_loaded, half * DMA + DMA)
                for p in range(NAT_SLOTS):
                    gather_pair(p)

            start(0, 1)
            with pool.Fori(0, HALVES) as half:
                lap = half + 1
                pool.wait_ge(prod_ready, lap * NT)
                for p in range(NAT_SLOTS, PAIRS):
                    if p >= GATHER_SEMS:
                        before = p - NAT_SLOTS if p >= GATHER_SEMS + NAT_SLOTS else p - GATHER_SEMS
                        pool.wait_ge(transposed, lap * PAIRS + before + 1)
                    gather_pair(p)
                start(half + 1, lap + 1)

        @block.scalar
        def _(act):
            act.sem_inc(emb_ready, PAIRS)
            act.sem_inc(q_hi_ready, FIELDS - 1)
            act.sem_inc(w_hi_placed, NW)
            act.sem_inc(z_copied, KT)
            act.sem_inc(h1_relu, NCH * H1 // P)
            act.sem_inc(h2_relu, NCH * H2 // P)
            act.sem_inc(y_copied, NCH)
            act.sem_inc(y_stored, NCH * DMA)
            act.wait_ge(ids_loaded, DMA)
            act.dma_start(w1_sb[:], w1).then_inc(mlp_weights_loaded, DMA)
            act.dma_start(w2_sb[:], w2).then_inc(mlp_weights_loaded, DMA)
            act.dma_start(w3_sb[:], w3).then_inc(mlp_weights_loaded, DMA)
            act.dma_start(b1_sb[:], b1).then_inc(mlp_weights_loaded, DMA)
            act.dma_start(b2_sb[:], b2).then_inc(mlp_weights_loaded, DMA)
            act.wait_ge(pad_set, 1)
            act.wait_ge(mlp_weights_loaded, 5 * DMA)

            def copy_pair(half, lap, p):
                act.wait_ge(transposed, lap * PAIRS + p + 1)
                if p == 0:
                    act.wait_ge(prod_ready, lap * NT)
                nc.scalar.activation(emb_t[:, p, :], e_ps[:], ACT.Copy).then_inc(emb_ready, 1)

            def hi_of_field(half, lap, c):
                act.wait_ge(emb_ready, lap * PAIRS + c // 2 + 1)
                act.wait_ge(u_ready, lap * NT + (first_tile(c - Q_SLOTS + 1) if c > Q_SLOTS else 0))
                nc.scalar.activation(q_parts[own(c), c % Q_SLOTS, 0, :], emb_t[own(c), c // 2, :], ACT.Copy
                                     ).then_inc(q_hi_ready, 1)

            def split_w(half, lap, j):
                raw = w_raw[:, j % RAW_SLOTS, :]
                act.wait_ge(w_raw_loaded[j % RAW_SLOTS], (half * (NW // RAW_SLOTS) + j // RAW_SLOTS + 1) * DMA)
                nc.scalar.activation(w_hi[:, j % RAW_SLOTS, :], raw, ACT.Copy)
                act.wait_ge(u_ready, lap * NT + max(j - W_SLOTS + 1, 0) * W_TILES)
                for part in range(2):
                    ins = nc.scalar.activation(w_parts[0:E, j % W_SLOTS, part * WC:part * WC + WC],
                                               raw[part * E:part * E + E, :], ACT.Copy)
                ins.then_inc(w_hi_placed, 1)

            def copy_z(half, lap, block_of_z):
                act.wait_ge(summed, lap * NG + min((block_of_z + 1) * SLOTS, NG))
                if block_of_z == 0:
                    act.wait_ge(h1_ready, lap * (NCH * H1 // P))
                rows = slice(0, DENSE_ROW if block_of_z == LAST else P)
                nc.scalar.activation(z_t[rows, block_of_z, :], z_ps[rows, :, :], ACT.Copy
                                     ).then_inc(z_copied, 1)

            def start(half, lap):
                copy_pair(half, lap, 1)
                hi_of_field(half, lap, 1)
                split_w(half, lap, 0)
                hi_of_field(half, lap, 2)
                split_w(half, lap, 1)
                hi_of_field(half, lap, 3)

            copy_pair(0, 1, 0)
            start(0, 1)
            with act.Fori(0, HALVES) as half:
                lap = half + 1
                act.dma_start(z_t[DENSE_ROW:DENSE_ROW + DENSE, LAST, :],
                              dense_t[:, bass.ds(half * HALF, HALF)]).then_inc(dense_loaded, DMA)
                for i in range(NT):
                    if i % W_TILES == 0 and i // W_TILES + RAW_SLOTS < NW:
                        split_w(half, lap, i // W_TILES + RAW_SLOTS)
                    for p in pairs_at[i]:
                        copy_pair(half, lap, p)
                    for c, n in fields_at[i]:
                        if n == 0:
                            hi_of_field(half, lap, c)
                    g, at = divmod(i, GROUP)
                    if at == 3 and g >= 1 and g % SLOTS == 0:
                        copy_z(half, lap, g // SLOTS - 1)
                copy_pair(half + 1, lap + 1, 0)
                copy_z(half, lap, LAST)
                start(half + 1, lap + 1)
                for n in range(NCH):
                    for m in range(H1 // P):
                        act.wait_ge(h1_ready, lap * (NCH * H1 // P) + n * (H1 // P) + m + 1)
                        nc.scalar.activation(h1[n][:, m, :], u_banks[:, m, :], ACT.Relu, bias=b1_sb[:, m:m + 1]
                                             ).then_inc(h1_relu, 1)
                    for m in range(H2 // P):
                        act.wait_ge(h2_ready, lap * (NCH * H2 // P) + n * (H2 // P) + m + 1)
                        nc.scalar.activation(h2[n][:, m, :], e_ps[:, m * CH:m * CH + CH], ACT.Relu,
                                             bias=b2_sb[:, m:m + 1]).then_inc(h2_relu, 1)
                    act.wait_ge(y_ready, lap * NCH + n + 1)
                    nc.scalar.activation(y_rows[n], z_ps[0:1, n, :], ACT.Copy).then_inc(y_copied, 1)
                    act.wait_ge(y_copied, lap * NCH + n + 1)
                    act.dma_start(out[:, bass.ds(half * HALF + n * CH, CH)], y_rows[n]).then_inc(y_stored, DMA)
            act.wait_ge(y_stored, (HALVES + 1) * NCH * DMA)

        @block.vector
        def _(dve):
            dve.sem_inc(q_lo_ready, FIELDS - 1)
            dve.sem_inc(w_lo_ready, NW)
            dve.sem_inc(prod_ready, NT)
            nc.vector.memset(z_t[96:P, LAST, :], 0.0).then_inc(pad_set, 1)

            def lo_of_field(half, lap, c, n):
                if n == 0:
                    dve.wait_ge(q_hi_ready, lap * (FIELDS - 1) + c)
                cols = slice(n * CH, n * CH + CH)
                ins = nc.vector.tensor_tensor(q_parts[own(c), c % Q_SLOTS, 1, cols], emb_t[own(c), c // 2, cols],
                                              q_parts[own(c), c % Q_SLOTS, 0, cols].bitcast(F32), ALU.subtract)
                if n == NCH - 1:
                    ins.then_inc(q_lo_ready, 1)

            def lo_of_w(half, lap, j):
                dve.wait_ge(w_hi_placed, lap * NW + j + 1)
                if j >= RAW_SLOTS:
                    i = j - RAW_SLOTS
                    dve.wait_ge(w_lo_placed[i % W_SLOTS], (half * (NW // W_SLOTS) + i // W_SLOTS + 1) * 2 * DMA)
                nc.vector.tensor_tensor(w_lo[:, j % RAW_SLOTS, :], w_raw[:, j % RAW_SLOTS, :],
                                        w_hi[:, j % RAW_SLOTS, :].bitcast(F32), ALU.subtract
                                        ).then_inc(w_lo_ready, 1)

            def start(half, lap):
                for c in (1, 2, 3):
                    for n in range(NCH):
                        lo_of_field(half, lap, c, n)
                    if c <= RAW_SLOTS:
                        lo_of_w(half, lap, c - 1)

            start(0, 1)
            with dve.Fori(0, HALVES) as half:
                lap = half + 1
                for i, (c, k) in enumerate(TILES):
                    for split, n in fields_at[i]:
                        lo_of_field(half, lap, split, n)
                    if k == 0:
                        dve.wait_ge(emb_ready, lap * PAIRS + c // 2 + 1)
                    if i == 3 * NCH:
                        dve.wait_ge(y_stored, lap * NCH * DMA)
                    if i % GROUP == 0:
                        dve.wait_ge(summed, lap * NG + max(i // GROUP - 1, 0))
                    dve.wait_ge(u_ready, lap * NT + i + 1)
                    nc.vector.tensor_tensor(prod[:, i % PROD_SLOTS, :],
                                            u[:, i % U_SLOTS, :, :].rearrange("p n x -> p (n x)"),
                                            emb_t[:, k, :], ALU.mult).then_inc(prod_ready, 1)
                    if i % W_TILES == 1 and i // W_TILES + RAW_SLOTS < NW:
                        lo_of_w(half, lap, i // W_TILES + RAW_SLOTS)
                start(half + 1, lap + 1)

        @block.tensor
        def _(pe):
            pe.sem_inc(transposed, PAIRS)
            pe.sem_inc(u_ready, NT)
            pe.sem_inc(summed, NG)
            pe.sem_inc(h1_ready, NCH * H1 // P)
            pe.sem_inc(h2_ready, NCH * H2 // P)
            pe.sem_inc(y_ready, NCH)
            pe.wait_ge(consts_loaded, 2 * DMA)

            def transpose_pair(half, lap, p):
                pe.wait_ge(gathered[p % GATHER_SEMS], (half * 2 + p // GATHER_SEMS + 1) * (2 * BT * DMA))
                pe.wait_ge(emb_ready, lap * PAIRS + p)
                if p == 2:
                    pe.wait_ge(h2_relu, lap * (NCH * H2 // P))
                for t in range(BT):
                    mm = nc.tensor.transpose(e_ps[:, t * P:t * P + P],
                                             gathered_rows(p)[:, t, :, :].rearrange("p a e -> p (a e)"), ident[:])
                mm.then_inc(transposed, 1)

            def contract(half, lap, i):
                c, k = TILES[i]
                j, at = divmod(i, W_TILES)
                if at == 0:
                    pe.wait_ge(w_hi_placed, lap * NW + j + 1)
                    pe.wait_ge(w_lo_placed[j % W_SLOTS], (half * (NW // W_SLOTS) + j // W_SLOTS + 1) * 2 * DMA)
                if k == 0:
                    pe.wait_ge(q_loaded[c % Q_SLOTS], q_loads(half, c) * DMA)
                pe.wait_ge(prod_ready, lap * NT + max(i - U_SLOTS + 1, 0))
                w = w_parts[:, j % W_SLOTS, at * P:at * P + P]
                for n in range(NCH):
                    cols = slice(n * CH, n * CH + CH)
                    nc.tensor.matmul(u[:, i % U_SLOTS, n, :], w, q_parts[:, c % Q_SLOTS, 0, cols],
                                     start=True, stop=False)
                    mm = nc.tensor.matmul(u[:, i % U_SLOTS, n, :], w, q_parts[:, c % Q_SLOTS, 1, cols],
                                          start=False, stop=True)
                mm.then_inc(u_ready, 1)

            def sum_group(half, lap, g, n):
                block_of_z, slot = divmod(g, SLOTS)
                if n == 0:
                    pe.wait_ge(prod_ready, lap * NT + GROUP * (g + 1))
                if n == 0 and slot == 0:
                    pe.wait_ge(z_copied, lap * KT + block_of_z)
                    if block_of_z == 0:
                        pe.wait_ge(y_copied, lap * NCH)
                last = slot == SLOTS - 1 or g == NG - 1
                for a in range(GROUP):
                    mm = nc.tensor.matmul(z_ps[32 * a:32 * a + 32, n, :], ones[:, 30 - 2 * slot:62 - 2 * slot],
                                          prod[:, (GROUP * g + a) % PROD_SLOTS, n * CH:n * CH + CH],
                                          start=(slot == 0), stop=last)
                if n == NCH - 1:
                    mm.then_inc(summed, 1)

            def first_layer(half, lap, n, m, blocks):
                for j in blocks:
                    if n == 0 and m == 0 and j == LAST:
                        pe.wait_ge(z_copied, lap * KT + KT)
                        pe.wait_ge(dense_loaded, half * DMA + DMA)
                    mm = nc.tensor.matmul(u_banks[:, m, :], w1_sb[:, j, m * P:m * P + P],
                                          z_t[:, j, n * CH:n * CH + CH], start=(j == 0), stop=(j == LAST))
                if LAST in blocks:
                    mm.then_inc(h1_ready, 1)

            def finish(half, lap):
                transpose_pair(half + 1, lap + 1, 0)
                pe.wait_ge(mlp_weights_loaded, 5 * DMA)
                pe.wait_ge(z_copied, lap * KT + LAST)
                pe.wait_ge(prod_ready, lap * NT + NT - 1)
                first_layer(half, lap, 0, 0, range(LAST))
                for n in range(NCH):
                    sum_group(half, lap, NG - 1, n)
                first_layer(half, lap, 0, 1, range(LAST))
                transpose_pair(half + 1, lap + 1, 1)
                for n in range(NCH):
                    for m in range(H1 // P):
                        if n >= 1:
                            pe.wait_ge(h1_relu, lap * (NCH * H1 // P) + (n - 1) * (H1 // P) + m + 1)
                        first_layer(half, lap, n, m, range(LAST if n == 0 and m < 2 else 0, KT))
                    if n == 0:
                        pe.wait_ge(emb_ready, (lap + 1) * PAIRS + NAT_SLOTS)
                    for m in range(H2 // P):
                        if n >= 1:
                            pe.wait_ge(h2_relu, lap * (NCH * H2 // P) + (n - 1) * (H2 // P) + m + 1)
                        for j in range(H1 // P):
                            if m == 0:
                                pe.wait_ge(h1_relu, lap * (NCH * H1 // P) + n * (H1 // P) + j + 1)
                            mm = nc.tensor.matmul(e_ps[:, m * CH:m * CH + CH], w2_sb[:, j, m * P:m * P + P],
                                                  h1[n][:, j, :], start=(j == 0), stop=(j == H1 // P - 1))
                        mm.then_inc(h2_ready, 1)
                    for j in range(H2 // P):
                        pe.wait_ge(h2_relu, lap * (NCH * H2 // P) + n * (H2 // P) + j + 1)
                        mm = nc.tensor.matmul(z_ps[0:1, n, :], w3_sb[:, j:j + 1], h2[n][:, j, :],
                                              start=(j == 0), stop=(j == H2 // P - 1))
                    mm.then_inc(y_ready, 1)

            for p in range(NAT_SLOTS):
                transpose_pair(0, 1, p)
            with pe.Fori(0, HALVES) as half:
                lap = half + 1
                for i in range(NT):
                    for p in pairs_at[i]:
                        transpose_pair(half, lap, p)
                    contract(half, lap, i)
                    g, at = divmod(i, GROUP)
                    if at % 2 == 1 and g >= 1:
                        sum_group(half, lap, g - 1, at // 2)
                finish(half, lap)


def kernel(**inputs):
    import concourse.bacc as bacc
    from concourse.bass_utils import run_bass_kernel_spmd

    a = {k: np.ascontiguousarray(v) for k, v in inputs.items()}

    param = np.concatenate([a["L0_rec_param"], np.zeros((E, 1, E), np.float32)], axis=1)
    order = [pair_index(2 * k + h, c) if 2 * k + h < c else -1 for c, k in TILES for h in range(2)]
    w_pairs = param[:, order, :].reshape(E, NW, 2, WC).transpose(1, 2, 0, 3).reshape(NW, P, WC)

    rows = z_rows()
    w1_ext = np.concatenate([a["W_top1"], np.zeros((1, H1), np.float32)], axis=0)
    rows[LAST, DENSE_ROW:DENSE_ROW + DENSE] = FIELDS * (FIELDS - 1) // 2 + np.arange(DENSE)
    w1 = w1_ext[rows].transpose(1, 0, 2)

    shifted_ones = np.zeros((P, 62), np.float32)
    shifted_ones[:E, 30] = shifted_ones[E:, 31] = 1.0

    ids = a["ids"].reshape(HALVES, BT, P, FIELDS).transpose(0, 2, 3, 1).reshape(HALVES, P, FIELDS * BT)

    arrays = {f"tbl_{c}": a[f"tbl_{c}"] for c in range(FIELDS)}
    arrays |= {
        "ids": np.concatenate([ids, np.zeros_like(ids[:1])], axis=0),
        "w_pairs": w_pairs,
        "w1": w1,
        "b1": a["b_top1"].reshape(H1 // P, P).T,
        "w2": a["W_top2"].reshape(H1 // P, P, H2).transpose(1, 0, 2),
        "b2": a["b_top2"].reshape(H2 // P, P).T,
        "w3": a["W_top3"].reshape(H2 // P, P).T,
        "dense_t": a["dense_ctx"].T,
        "identity": np.eye(P, dtype=np.float32),
        "shifted_ones": shifted_ones,
    }
    nc = bacc.Bacc("TRN2", target_bir_lowering=False, num_devices=1)
    feeds, aps = {}, {}
    for name, array in arrays.items():
        array = np.ascontiguousarray(array)
        feeds[f"in_{name}"] = array
        aps[name] = nc.dram_tensor(f"in_{name}", array.shape, mybir.dt.from_np(array.dtype),
                                   kind="ExternalInput").ap()
    out = nc.dram_tensor("y", (1, BATCH), F32, kind="ExternalOutput").ap()
    tables = [aps.pop(f"tbl_{c}") for c in range(FIELDS)]
    build(nc, tables, out=out, **aps)
    r = run_bass_kernel_spmd(nc, [feeds], core_ids=[0])
    return r.results[0]["y"].reshape(BATCH, 1)
```
